# Optimizing a Trainium2 kernel written in Bass

```python
import numpy as np
import jax
import jax.numpy as jnp

def _softmax(x, axis=-1):
    return jax.nn.softmax(x, axis=axis)

def _gelu(x):
    return jax.nn.gelu(x, approximate=True)

def _silu(x):
    return jax.nn.silu(x)

def _sigmoid(x):
    return jax.nn.sigmoid(x)

def _layernorm(x, axis=-1, eps=1e-05):
    m = jnp.mean(x, axis=axis, keepdims=True)
    v = jnp.var(x, axis=axis, keepdims=True)
    return (x - m) / jnp.sqrt(v + eps)

def _scatter_add(tgt, idx, src, axis=0):
    return tgt.at[idx].add(src)

def _segment_sum(src, seg, n):
    return jax.ops.segment_sum(src, seg, n)
kernel_name = 'mk_gnn_preln_d2_gnn_r8_247c67'

def setup_inputs(seed: int=0):
    np.random.seed(seed)
    _w = jnp.asarray

    def _rec_inputs():
        import jax
        import jax.numpy as jnp
        _gk = jax.random.key(seed)
        x = -0.000202 + 1 * jax.random.normal(jax.random.fold_in(_gk, 1), (12500, 128), jnp.float32)
        src = jax.random.randint(jax.random.fold_in(_gk, 2), (200000,), 0, 12500, jnp.int32)
        dst = jnp.minimum((12500 * jax.random.uniform(jax.random.fold_in(_gk, 3), (200000,)) ** 2.0).astype(jnp.int32), 99999)
        _o = jnp.argsort(dst, stable=True)
        src = src[_o]
        dst = dst[_o]
        edge_attr_16 = 0.000254156 + 0.999948 * jax.random.normal(jax.random.fold_in(_gk, 12), (200000, 16), jnp.float32)
        return (x, src, dst, edge_attr_16)
    x, src, dst, edge_attr_16 = _rec_inputs()

    def _L0_gnn_setup():
        import jax, jax.numpy as jnp
        import numpy as np
        N_NODES = 6250
        N_EDGES = 100000
        D = 128
        key = jax.random.key(seed)
        k1, k2, k3, k4, k5 = jax.random.split(key, 5)
        N = jax.random.normal(k1, (N_NODES, D), dtype=jnp.float32)
        W1 = jax.random.normal(k2, (D, D), dtype=jnp.float32) * (1.0 / np.sqrt(D))
        w2 = jax.random.normal(k3, (D,), dtype=jnp.float32) * (1.0 / np.sqrt(D))
        src = jax.random.randint(k4, (N_EDGES,), 0, N_NODES, dtype=jnp.int32)
        dst = jax.random.randint(k5, (N_EDGES,), 0, N_NODES, dtype=jnp.int32)
        return {'N': N, 'W1': W1, 'w2': w2, 'src': src, 'dst': dst}
    _L0_gnn_all = _L0_gnn_setup()
    _L0_gnn_in = {k: v for k, v in _L0_gnn_all.items() if k in ('W1', 'w2')}
    del _L0_gnn_all

    def _L1_gnn_setup():
        import jax, jax.numpy as jnp
        import numpy as np
        N_NODES = 6250
        N_EDGES = 100000
        IN_CH = 128
        HIDDEN = 16
        HEADS = 8
        OUT_CH = 128
        EDGE_DIM = 16

        def _lin_params(key, fan_in, fan_out, bias=True):
            k1, k2 = jax.random.split(key)
            s = 1.0 / np.sqrt(fan_in)
            W = jax.random.uniform(k1, (fan_in, fan_out), jnp.float32, -s, s)
            if bias:
                b = jax.random.uniform(k2, (fan_out,), jnp.float32, -s, s)
                return (W, b)
            return W

        def transformer_conv(x, src, dst, edge_attr, Wq, bq, Wk, bk, Wv, bv, We, Ws, bs, heads, concat):
            N = x.shape[0]
            E = src.shape[0]
            C = Wq.shape[1] // heads
            q = (x @ Wq + bq).reshape(N, heads, C)
            k = (x @ Wk + bk).reshape(N, heads, C)
            v = (x @ Wv + bv).reshape(N, heads, C)
            e = (edge_attr @ We).reshape(E, heads, C)
            key_e = k[src] + e
            alpha = jnp.sum(q[dst] * key_e, axis=-1) / jnp.sqrt(jnp.asarray(C, x.dtype))
            m = jax.ops.segment_max(alpha, dst, num_segments=N)
            p = jnp.exp(alpha - m[dst])
            denom = jax.ops.segment_sum(p, dst, num_segments=N)
            w = p / (denom[dst] + 1e-16)
            msg = (v[src] + e) * w[..., None]
            agg = jax.ops.segment_sum(msg.reshape(E, heads * C), dst, num_segments=N).reshape(N, heads, C)
            out = agg.reshape(N, heads * C) if concat else agg.mean(axis=1)
            return out + (x @ Ws + bs)
        key = jax.random.key(seed)
        ks = jax.random.split(key, 16)
        x = jax.random.normal(ks[0], (N_NODES, IN_CH), jnp.float32)
        edge_index = jax.random.randint(ks[1], (2, N_EDGES), 0, N_NODES, jnp.int64)
        edge_attr = jax.random.normal(ks[2], (N_EDGES, EDGE_DIM), jnp.float32)
        HC0 = HEADS * HIDDEN
        Wq0, bq0 = _lin_params(ks[3], IN_CH, HC0)
        Wk0, bk0 = _lin_params(ks[4], IN_CH, HC0)
        Wv0, bv0 = _lin_params(ks[5], IN_CH, HC0)
        We0 = _lin_params(ks[6], EDGE_DIM, HC0, bias=False)
        Ws0, bs0 = _lin_params(ks[7], IN_CH, HC0)
        Wq1, bq1 = _lin_params(ks[8], HC0, OUT_CH)
        Wk1, bk1 = _lin_params(ks[9], HC0, OUT_CH)
        Wv1, bv1 = _lin_params(ks[10], HC0, OUT_CH)
        We1 = _lin_params(ks[11], EDGE_DIM, OUT_CH, bias=False)
        Ws1, bs1 = _lin_params(ks[12], HC0, OUT_CH)
        return dict(x=x, edge_index=edge_index, edge_attr=edge_attr, Wq0=Wq0, bq0=bq0, Wk0=Wk0, bk0=bk0, Wv0=Wv0, bv0=bv0, We0=We0, Ws0=Ws0, bs0=bs0, Wq1=Wq1, bq1=bq1, Wk1=Wk1, bk1=bk1, Wv1=Wv1, bv1=bv1, We1=We1, Ws1=Ws1, bs1=bs1)
    _L1_gnn_all = _L1_gnn_setup()
    _L1_gnn_in = {k: v for k, v in _L1_gnn_all.items() if k in ('Wq0', 'bq0', 'Wk0', 'bk0', 'Wv0', 'bv0', 'We0', 'Ws0', 'bs0', 'Wq1', 'bq1', 'Wk1', 'bk1', 'Wv1', 'bv1', 'We1', 'Ws1', 'bs1')}
    del _L1_gnn_all
    return {'x': x, 'src': src, 'dst': dst, 'edge_attr_16': edge_attr_16, 'L0_gnn_W1': _L0_gnn_in['W1'], 'L0_gnn_w2': _L0_gnn_in['w2'], 'L1_gnn_Wq0': _L1_gnn_in['Wq0'], 'L1_gnn_bq0': _L1_gnn_in['bq0'], 'L1_gnn_Wk0': _L1_gnn_in['Wk0'], 'L1_gnn_bk0': _L1_gnn_in['bk0'], 'L1_gnn_Wv0': _L1_gnn_in['Wv0'], 'L1_gnn_bv0': _L1_gnn_in['bv0'], 'L1_gnn_We0': _L1_gnn_in['We0'], 'L1_gnn_Ws0': _L1_gnn_in['Ws0'], 'L1_gnn_bs0': _L1_gnn_in['bs0'], 'L1_gnn_Wq1': _L1_gnn_in['Wq1'], 'L1_gnn_bq1': _L1_gnn_in['bq1'], 'L1_gnn_Wk1': _L1_gnn_in['Wk1'], 'L1_gnn_bk1': _L1_gnn_in['bk1'], 'L1_gnn_Wv1': _L1_gnn_in['Wv1'], 'L1_gnn_bv1': _L1_gnn_in['bv1'], 'L1_gnn_We1': _L1_gnn_in['We1'], 'L1_gnn_Ws1': _L1_gnn_in['Ws1'], 'L1_gnn_bs1': _L1_gnn_in['bs1']}

def reference(x, src, dst, edge_attr_16, L0_gnn_W1, L0_gnn_w2, L1_gnn_Wq0, L1_gnn_bq0, L1_gnn_Wk0, L1_gnn_bk0, L1_gnn_Wv0, L1_gnn_bv0, L1_gnn_We0, L1_gnn_Ws0, L1_gnn_bs0, L1_gnn_Wq1, L1_gnn_bq1, L1_gnn_Wk1, L1_gnn_bk1, L1_gnn_Wv1, L1_gnn_bv1, L1_gnn_We1, L1_gnn_Ws1, L1_gnn_bs1):
    import jax
    import jax.numpy as jnp

    def _L0_gnn_ref(N, W1, w2, src, dst):
        import jax, jax.numpy as jnp
        import numpy as np
        N_NODES = 6250
        N_EDGES = 100000
        D = 128
        n_nodes = N.shape[0]
        logit = jnp.tanh(N @ W1.T) @ w2
        e = logit[src]
        seg_max = jax.ops.segment_max(e, dst, num_segments=n_nodes)
        seg_max = jnp.where(jnp.isfinite(seg_max), seg_max, 0.0)
        ex = jnp.exp(e - seg_max[dst])
        denom = jax.ops.segment_sum(ex, dst, num_segments=n_nodes)
        a = ex / denom[dst]
        Np = jax.ops.segment_sum(a[:, None] * N[src], dst, num_segments=n_nodes)
        return Np

    def _L1_gnn_ref(x, edge_index, edge_attr, Wq0, bq0, Wk0, bk0, Wv0, bv0, We0, Ws0, bs0, Wq1, bq1, Wk1, bk1, Wv1, bv1, We1, Ws1, bs1):
        import jax, jax.numpy as jnp
        import numpy as np
        N_NODES = 6250
        N_EDGES = 100000
        IN_CH = 128
        HIDDEN = 16
        HEADS = 8
        OUT_CH = 128
        EDGE_DIM = 16

        def _lin_params(key, fan_in, fan_out, bias=True):
            k1, k2 = jax.random.split(key)
            s = 1.0 / np.sqrt(fan_in)
            W = jax.random.uniform(k1, (fan_in, fan_out), jnp.float32, -s, s)
            if bias:
                b = jax.random.uniform(k2, (fan_out,), jnp.float32, -s, s)
                return (W, b)
            return W

        def transformer_conv(x, src, dst, edge_attr, Wq, bq, Wk, bk, Wv, bv, We, Ws, bs, heads, concat):
            N = x.shape[0]
            E = src.shape[0]
            C = Wq.shape[1] // heads
            q = (x @ Wq + bq).reshape(N, heads, C)
            k = (x @ Wk + bk).reshape(N, heads, C)
            v = (x @ Wv + bv).reshape(N, heads, C)
            e = (edge_attr @ We).reshape(E, heads, C)
            key_e = k[src] + e
            alpha = jnp.sum(q[dst] * key_e, axis=-1) / jnp.sqrt(jnp.asarray(C, x.dtype))
            m = jax.ops.segment_max(alpha, dst, num_segments=N)
            p = jnp.exp(alpha - m[dst])
            denom = jax.ops.segment_sum(p, dst, num_segments=N)
            w = p / (denom[dst] + 1e-16)
            msg = (v[src] + e) * w[..., None]
            agg = jax.ops.segment_sum(msg.reshape(E, heads * C), dst, num_segments=N).reshape(N, heads, C)
            out = agg.reshape(N, heads * C) if concat else agg.mean(axis=1)
            return out + (x @ Ws + bs)
        src, dst = (edge_index[0], edge_index[1])
        h = transformer_conv(x, src, dst, edge_attr, Wq0, bq0, Wk0, bk0, Wv0, bv0, We0, Ws0, bs0, heads=HEADS, concat=True)
        h = jax.nn.relu(h)
        out = transformer_conv(h, src, dst, edge_attr, Wq1, bq1, Wk1, bk1, Wv1, bv1, We1, Ws1, bs1, heads=1, concat=False)
        return out
    edge_index = jnp.stack([src, dst])
    h = jnp.maximum(_layernorm(x, axis=-1), 0.0)
    x = x + _L0_gnn_ref(h, L0_gnn_W1, L0_gnn_w2, src, dst)
    h = jnp.maximum(_layernorm(x, axis=-1), 0.0)
    x = x + _L1_gnn_ref(h, edge_index, edge_attr_16, L1_gnn_Wq0, L1_gnn_bq0, L1_gnn_Wk0, L1_gnn_bk0, L1_gnn_Wv0, L1_gnn_bv0, L1_gnn_We0, L1_gnn_Ws0, L1_gnn_bs0, L1_gnn_Wq1, L1_gnn_bq1, L1_gnn_Wk1, L1_gnn_bk1, L1_gnn_Wv1, L1_gnn_bv1, L1_gnn_We1, L1_gnn_Ws1, L1_gnn_bs1)
    return x

_drawn_inputs = setup_inputs


def setup_inputs(seed=0):
    import zlib

    import numpy as np

    out = dict(_drawn_inputs(seed))
    spreads = {}
    factors = {'L1_gnn_bq0': 8.0,
     'L1_gnn_Wk0': 5.486,
     'L1_gnn_bk0': 8.0,
     'L1_gnn_Wq1': 2.832,
     'L1_gnn_bq1': 8.0,
     'L1_gnn_Wk1': 8.0,
     'L1_gnn_bk1': 8.0}
    for name, (base, spread) in spreads.items():
        noise = np.random.default_rng([zlib.crc32(name.encode()), seed]).standard_normal(out[name].shape)
        drawn = base * np.exp(spread * noise) if base else spread * noise
        out[name] = jnp.asarray(drawn.astype(out[name].dtype))
    for name, factor in factors.items():
        out[name] = (out[name] * factor).astype(out[name].dtype)
    return out
```

```python
from contextlib import ExitStack

import concourse.bass as bass
from concourse import mybir

F32 = mybir.dt.float32
I32 = mybir.dt.int32
U32 = mybir.dt.uint32
BF16 = mybir.dt.bfloat16
ALU = mybir.AluOpType
ACT = mybir.ActivationFunctionType
AX = mybir.AxisListType
ds = bass.ds

P = 128
N_NODES = 12500
N_EDGES = 200000
D = 128
HEADS = 8
HEAD_DIM = D // HEADS
EDGE_DIM = 16
NODE_TILES = -(-N_NODES // P)
NODES = NODE_TILES * P
SLOTS = NODE_TILES + 1
J = 4
BLOCKS = -(-N_EDGES // (J * P))
EDGES = BLOCKS * J * P
CHUNKS = -(-BLOCKS * J // P)
EDGE_TILES = CHUNKS * P
ITEMS = BLOCKS + NODE_TILES - 1
U = 8
PACK = 4
GROUPS = ITEMS // PACK
QB = 4
PAD_DST = NODES - 1
ROWS_B = 7
BATCHES = NODE_TILES // ROWS_B
TAIL = EDGE_DIM + 1
ACC_W = D + TAIL
HW = HEAD_DIM + 1
BIG = 2.0 ** 100
LN_EPS = 1e-5
DEN_EPS = 1e-16
assert ITEMS % U == 0 and NODE_TILES % ROWS_B == 0 and BATCHES % 2 == 0


def rolled(eng, total, unroll, lag, step, begin=None, peel=2):
    assert lag <= unroll
    rounds = total // unroll
    for r in range(peel):
        if begin:
            begin(r)
        for u in range(unroll):
            step(r * unroll + u, u)
    with eng.Fori(peel, rounds) as r:
        if begin:
            begin(r)
        for u in range(unroll):
            step(r * unroll + u, u)
    for n in range(rounds * unroll, total + lag):
        if begin and n % unroll == 0:
            begin(n // unroll)
        step(n, n % unroll)


def settle(g, eng):
    eng.sem_inc(g.settled, 1)


def has(n, total):
    return not isinstance(n, int) or 0 <= n < total


class Signal:

    def __init__(self, sem):
        self.sem, self.base = sem, 0

    def wait(self, eng, n):
        if isinstance(n, int) and self.base + n + 1 <= 0:
            return
        eng.wait_ge(self.sem, n + (self.base + 1))


class Program:

    def __init__(self, nc, t, ctx):
        self.nc, self.t, self.ctx = nc, t, ctx


def build(nc, t):
    with ExitStack() as ctx:
        g = Program(nc, t, ctx)
        buffers(g)
        prepare(g)
        g.acc = sb(g, ctx, "acc", [P, SLOTS, ACC_W])
        g.run_max = sb(g, ctx, "run_max", [P, SLOTS, HEADS])
        signals(g)
        hidden_stage(g)
        edge_signals(g)
        g.acc_clear, g.w_edge_clear, g.w_edge_loaded = (sem(g, k) for k in ("acc_clear", "w_edge_clear", "w_edge_loaded"))
        edge_stage(g, "pool", g.pool_rows, D + 2, 1, 8)
        project_stage(g)
        edge_stage(g, "multi", g.kv_rows, 2 * D, HEADS, 4)
        fold_stage(g)
        edge_stage(g, "single", g.h2_rows, D, 1, 8)
        output_stage(g)


def sb(g, stack, name, shape, dt=F32):
    return stack.enter_context(g.nc.sbuf_tensor(name, shape, dt))


def pb(g, stack, name, shape):
    return stack.enter_context(g.nc.psum_tensor(name, shape, F32))


def sem(g, name):
    return g.ctx.enter_context(g.nc.semaphore(name))


def buffers(g):
    def scratch(name, shape):
        return g.nc.dram_tensor(name, shape, F32, kind="Internal").ap()

    g.pool_rows = scratch("pool_rows", [NODES, D + 2])
    g.kv_rows = scratch("kv_rows", [NODES, 2 * D])
    g.h2_rows = scratch("h2_rows", [NODES, D])
    g.x1_rows = scratch("x1_rows", [NODES, D])
    g.skip1_rows = scratch("skip1_rows", [NODES, D])
    g.skip2_rows = scratch("skip2_rows", [NODES, D])
    g.resets = scratch("resets", [EDGE_TILES, P])
    g.row_scratch = scratch("row_scratch", [2, 392])
    g.parts = {W: g.nc.dram_tensor(f"query_parts{W}", [SLOTS * P, 3 * W], BF16, kind="Internal").ap()
               for W in (D, ACC_W)}
    ctx = g.ctx
    g.ident = sb(g, ctx, "ident", [P, P])
    g.tile_base = sb(g, ctx, "tile_base", [P, SLOTS])
    g.dst_cols = sb(g, ctx, "dst_cols", [P, BLOCKS * J])
    g.last_cols = sb(g, ctx, "last_cols", [P, BLOCKS * J])
    g.src_cols = sb(g, ctx, "src_cols", [P, BLOCKS * J], U32)
    g.item_words = sb(g, ctx, "item_words", [1, GROUPS], I32)
    g.block_ends = sb(g, ctx, "block_ends", [1, 392], I32)
    g.ident_b = sb(g, ctx, "ident_b", [P, P], BF16)
    g.iota_b = sb(g, ctx, "iota_b", [P, P], BF16)
    g.neg_big = sb(g, ctx, "neg_big", [P, 1])
    g.ln_eps = sb(g, ctx, "ln_eps", [P, 1])


def prepare(g):
    nc, t = g.nc, g.t
    ident, tile_base, neg_big, ln_eps = g.ident, g.tile_base, g.neg_big, g.ln_eps
    dst_cols, last_cols, src_cols = g.dst_cols, g.last_cols, g.src_cols
    item_words, block_ends, resets, row_scratch = g.item_words, g.block_ends, g.resets, g.row_scratch
    g.settled = sem(g, "settled")
    s_const = sem(g, "const_ready")
    s_load = sem(g, "prep_loaded")
    s_dve = sem(g, "prep_dve")
    s_pe = sem(g, "prep_pe")
    s_store = sem(g, "prep_stored")

    with ExitStack() as ph:
        dst_i = sb(g, ph, "dst_i", [P, CHUNKS, P], I32)
        src_i = sb(g, ph, "src_i", [P, CHUNKS, P], I32)
        dst_f = sb(g, ph, "dst_f", [P, CHUNKS, P])
        src_f = sb(g, ph, "src_f", [P, CHUNKS, P])
        edge_q = sb(g, ph, "edge_q", [P, CHUNKS, P + 1])
        reset_f = sb(g, ph, "reset_f", [P, CHUNKS, P])
        ends_i = sb(g, ph, "ends_i", [1, 2, 392], I32)
        tile_i = sb(g, ph, "tile_i", [1, 2, 392], I32)
        lo = sb(g, ph, "lo", [1, 392])
        hi = sb(g, ph, "hi", [1, 392])
        cand = sb(g, ph, "cand", [1, 392])
        cnt = sb(g, ph, "cnt", [1, 392])
        zeros = sb(g, ph, "zeros", [1, 392])
        end = sb(g, ph, "end", [1, 392])
        shift = sb(g, ph, "shift", [1, 393])
        jump = sb(g, ph, "jump", [1, 392])
        end_p = sb(g, ph, "end_p", [98, 4])
        jump_p = sb(g, ph, "jump_p", [98, 4])
        iota_i = sb(g, ph, "iota_i", [98, ITEMS], I32)
        iota_f = sb(g, ph, "iota_f", [98, ITEMS])
        passed = sb(g, ph, "passed", [98, 4, ITEMS])
        ones_c = sb(g, ph, "ones_c", [98, 1])
        item_b = sb(g, ph, "item_b", [1, ITEMS])
        item_t = sb(g, ph, "item_t", [1, ITEMS])
        item_y = sb(g, ph, "item_y", [1, ITEMS])
        step_y = sb(g, ph, "step_y", [1, GROUPS, 3])
        word = sb(g, ph, "word", [1, GROUPS])
        iota_ni = sb(g, ph, "iota_ni", [P, P], I32)
        base_i = sb(g, ph, "base_i", [P, SLOTS], I32)
        ps_t = [pb(g, ph, f"ps_t{k}", [P, 512]) for k in range(4)]
        ps_b = pb(g, ph, "ps_b", [P, 512])
        ps_n = pb(g, ph, "ps_n", [P, 512])
        block = ph.enter_context(nc.Block())

        @block.sync
        def _(sp):
            sp.dma_start(dst_i[:], t["dst"].rearrange("(c p) n -> p c n", p=P)).then_inc(s_load, 16)
            sp.dma_start(src_i[:], t["src"].rearrange("(c p) n -> p c n", p=P)).then_inc(s_load, 16)
            with nc.allow_non_contiguous_dma(reason="one word per block"):
                blocks = t["dst"].rearrange("(b j) n -> b (j n)", j=J)
                sp.dma_start(ends_i[0:1, 0, 0:BLOCKS], blocks[0:BLOCKS, 0:1].rearrange("b a -> a b"))\
                  .then_inc(s_load, 16)
                sp.dma_start(ends_i[0:1, 1, 0:BLOCKS],
                             blocks[0:BLOCKS, J * P - 1:J * P].rearrange("b a -> a b")).then_inc(s_load, 16)
            sp.wait_ge(s_dve, 4)
            sp.dma_start(resets.rearrange("(c p) n -> p c n", p=P), reset_f[:]).then_inc(s_store, 16)
            sp.wait_ge(s_dve, 15)
            sp.dma_start(row_scratch[0:1, :], end[:]).then_inc(s_store, 16)
            sp.dma_start(row_scratch[1:2, :], jump[:]).then_inc(s_store, 16)
            sp.wait_ge(s_store, 48)
            sp.dma_start(end_p[:], row_scratch[0, :].rearrange("(p k) -> p k", k=4)).then_inc(s_load, 16)
            sp.dma_start(jump_p[:], row_scratch[1, :].rearrange("(p k) -> p k", k=4)).then_inc(s_load, 16)
            sp.wait_ge(s_load, 96)

        @block.gpsimd
        def _(pool):
            pool.memset(ident[:], 0.0).then_inc(s_const, 1)
            pool.iota(iota_ni[:], pattern=[[1, P]], base=0, channel_multiplier=0).then_inc(s_const, 1)
            pool.iota(base_i[:], pattern=[[P, SLOTS]], base=0, channel_multiplier=0).then_inc(s_const, 1)
            pool.iota(iota_i[:], pattern=[[1, ITEMS]], base=0, channel_multiplier=0).then_inc(s_const, 1)
            pool.memset(neg_big[:], -BIG).then_inc(s_const, 1)
            pool.memset(ln_eps[:], LN_EPS).then_inc(s_const, 1)
            pool.memset(ones_c[:], 1.0).then_inc(s_const, 1)
            pool.wait_ge(s_const, 7)
            pool.affine_select(out=ident[:], in_=ident[:], compare_op=ALU.not_equal, fill=1.0, base=0,
                               pattern=[[-1, P]], channel_multiplier=1).then_inc(s_const, 1)

        @block.vector
        def _(dve):
            v = nc.vector
            dve.wait_ge(s_load, 64)
            v.tensor_copy(dst_f[:], dst_i[:]).then_inc(s_dve, 1)
            v.memset(edge_q[:], 1.0).then_inc(s_dve, 1)
            dve.wait_ge(s_dve, 2)
            v.tensor_tensor(out=edge_q[:, :, 1:P], in0=dst_f[:, :, 1:P], in1=dst_f[:, :, 0:P - 1],
                            op=ALU.not_equal).then_inc(s_dve, 1)
            dve.wait_ge(s_dve, 3)
            v.tensor_scalar(reset_f[:], edge_q[:, :, 0:P], -BIG, None, ALU.mult).then_inc(s_dve, 1)
            v.tensor_scalar(tile_i[0:1, :, 0:BLOCKS], ends_i[0:1, :, 0:BLOCKS], 7, None,
                            ALU.logical_shift_right).then_inc(s_dve, 1)
            v.tensor_copy(src_f[:], src_i[:]).then_inc(s_dve, 1)
            dve.wait_ge(s_dve, 6)
            v.tensor_copy(lo[0:1, 1:BLOCKS], tile_i[0:1, 0, 1:BLOCKS])
            v.tensor_copy(hi[0:1, 0:BLOCKS], tile_i[0:1, 1, 0:BLOCKS])
            v.memset(lo[0:1, 0:1], 0.0)
            v.memset(zeros[:], 0.0)
            v.memset(lo[0:1, BLOCKS:BLOCKS + 1], float(NODE_TILES)).then_inc(s_dve, 1)
            dve.wait_ge(s_dve, 7)
            v.tensor_scalar(cand[0:1, 0:BLOCKS], lo[0:1, 1:BLOCKS + 1], -1.0, None, ALU.add).then_inc(s_dve, 1)
            dve.wait_ge(s_dve, 8)
            v.tensor_tensor(out=hi[0:1, 0:BLOCKS], in0=hi[0:1, 0:BLOCKS], in1=cand[0:1, 0:BLOCKS],
                            op=ALU.max).then_inc(s_dve, 1)
            dve.wait_ge(s_dve, 9)
            v.scalar_tensor_tensor(out=cnt[0:1, 0:BLOCKS], in0=hi[0:1, 0:BLOCKS], scalar=1.0,
                                   in1=lo[0:1, 0:BLOCKS], op0=ALU.add, op1=ALU.subtract).then_inc(s_dve, 1)
            dve.wait_ge(s_dve, 10)
            v.tensor_tensor_scan(end[0:1, 0:BLOCKS], cnt[0:1, 0:BLOCKS], zeros[0:1, 0:BLOCKS], 0.0,
                                 ALU.add, ALU.add).then_inc(s_dve, 1)
            dve.wait_ge(s_dve, 11)
            v.tensor_tensor(out=shift[0:1, 0:BLOCKS], in0=hi[0:1, 0:BLOCKS], in1=end[0:1, 0:BLOCKS],
                            op=ALU.subtract)
            v.memset(end[0:1, BLOCKS:392], 1e6)
            v.tensor_scalar(shift[0:1, BLOCKS:BLOCKS + 1], end[0:1, BLOCKS - 1:BLOCKS], -1.0,
                            float(NODE_TILES), ALU.mult, ALU.add).then_inc(s_dve, 1)
            dve.wait_ge(s_dve, 12)
            v.tensor_scalar(shift[0:1, 0:BLOCKS], shift[0:1, 0:BLOCKS], 1.0, None, ALU.add).then_inc(s_dve, 1)
            dve.wait_ge(s_dve, 13)
            v.tensor_tensor(out=jump[0:1, 0:BLOCKS], in0=shift[0:1, 1:BLOCKS + 1],
                            in1=shift[0:1, 0:BLOCKS], op=ALU.subtract)
            v.memset(jump[0:1, BLOCKS:392], 0.0).then_inc(s_dve, 1)
            v.tensor_copy(block_ends[:], end[:]).then_inc(s_dve, 1)
            dve.wait_ge(s_const, 8)
            v.tensor_copy(g.iota_b[:], iota_ni[:])
            v.tensor_copy(g.ident_b[:], ident[:])
            v.tensor_copy(tile_base[:], base_i[:])
            v.tensor_copy(iota_f[:], iota_i[:])
            v.memset(item_y[:], 0.0).then_inc(s_dve, 1)
            for k in range(3 * CHUNKS):
                what, c = divmod(k, CHUNKS)
                dest = (dst_cols, last_cols, src_cols)[what]
                w = min(P, BLOCKS * J - c * P)
                dve.wait_ge(s_pe, k + 1)
                v.tensor_copy(dest[:, c * P:c * P + w], ps_t[k % 4][:, 0:w]).then_inc(s_dve, 1)
            done = 16 + 3 * CHUNKS
            dve.wait_ge(s_load, 96)
            dve.wait_ge(s_dve, 16)
            for k in range(4):
                v.tensor_scalar(passed[:, k, :], iota_f[:], end_p[:, k:k + 1], None, ALU.is_ge)\
                 .then_inc(s_dve, 1)
            dve.wait_ge(s_pe, 3 * CHUNKS + 1)
            v.tensor_scalar(item_b[:], ps_b[0:1, 0:ITEMS], float(BLOCKS - 1), None, ALU.min).then_inc(s_dve, 1)
            v.tensor_tensor(out=item_t[:], in0=ps_n[0:1, 0:ITEMS], in1=iota_f[0:1, :], op=ALU.add)\
             .then_inc(s_dve, 1)
            dve.wait_ge(s_dve, done + 6)
            v.tensor_scalar(item_t[:], item_t[:], float(NODE_TILES), None, ALU.min).then_inc(s_dve, 1)
            dve.wait_ge(s_dve, done + 7)
            v.scalar_tensor_tensor(out=item_y[:], in0=item_t[:], scalar=2.0, in1=item_b[:],
                                   op0=ALU.mult, op1=ALU.add).then_inc(s_dve, 1)
            b4 = item_b[:].rearrange("a (g u) -> a g u", u=PACK)
            t4 = item_t[:].rearrange("a (g u) -> a g u", u=PACK)
            y4 = item_y[:].rearrange("a (g u) -> a g u", u=PACK)
            v.scalar_tensor_tensor(out=word[:], in0=t4[:, :, 0], scalar=512.0, in1=b4[:, :, 0],
                                   op0=ALU.mult, op1=ALU.add).then_inc(s_dve, 1)
            dve.wait_ge(s_dve, done + 9)
            v.tensor_tensor(out=step_y[:], in0=y4[:, :, 1:4], in1=y4[:, :, 0:3], op=ALU.subtract)\
             .then_inc(s_dve, 1)
            for k in range(3):
                dve.wait_ge(s_dve, done + 10 + k)
                v.scalar_tensor_tensor(out=word[:], in0=step_y[:, :, k], scalar=float(1 << (16 + 2 * k)),
                                       in1=word[:], op0=ALU.mult, op1=ALU.add).then_inc(s_dve, 1)
            dve.wait_ge(s_dve, done + 13)
            v.tensor_copy(item_words[:], word[:]).then_inc(s_dve, 1)

        @block.tensor
        def _(pe):
            pe.wait_ge(s_const, 8)
            for k in range(3 * CHUNKS):
                what, c = divmod(k, CHUNKS)
                src = (dst_f[:, c, :], edge_q[:, c, 1:P + 1], src_f[:, c, :])[what]
                pe.wait_ge(s_dve, max(6, 16 + k - 3))
                nc.tensor.transpose(ps_t[k % 4][:, 0:P], src, ident[:]).then_inc(s_pe, 1)
            pe.wait_ge(s_dve, 16 + 3 * CHUNKS + 4)
            for k in range(4):
                nc.tensor.matmul(ps_b[0:1, 0:ITEMS], ones_c[:], passed[:, k, :], start=(k == 0), stop=(k == 3))
            for k in range(4):
                last = nc.tensor.matmul(ps_n[0:1, 0:ITEMS], jump_p[:, k:k + 1], passed[:, k, :],
                                        start=(k == 0), stop=(k == 3))
            last.then_inc(s_pe, 1)


def rows_of(dram, k):
    return dram.rearrange("(t p) n -> p t n", p=P)[:, ds(k * ROWS_B, ROWS_B), :]


def signals(g):
    g.loaded = [sem(g, f"rows_loaded{k}") for k in range(2)]
    g.loaded2 = [sem(g, f"rows2_loaded{k}") for k in range(2)]
    g.stored = [sem(g, f"rows_stored{k}") for k in range(2)]
    names = ("acc_read", "x_sum", "stats", "var", "std", "rstd", "normal", "hidden", "turned",
             "turned_sb", "product", "product_read", "tanh", "weighed", "q_turned", "q_turned_sb",
             "query_done", "part", "rest", "den", "extra")
    g.dense = {k: Signal(sem(g, "dense_" + k)) for k in names}
    g.weights_loaded = sem(g, "weights_loaded")
    g.weights_turned = sem(g, "weights_turned")
    g.weights_ready = sem(g, "weights_ready")


def hidden_stage(g):
    nc, t, ident, acc, run_max, ln_eps = g.nc, g.t, g.ident, g.acc, g.run_max, g.ln_eps
    d_in, d_out, D_ = g.loaded, g.stored, g.dense
    s_w, s_wpe, s_wdve = g.weights_loaded, g.weights_turned, g.weights_ready
    V, S_, T_ = nc.vector, nc.scalar, nc.tensor

    with ExitStack() as ph:
        xb = sb(g, ph, "xb0", [P, 2, ROWS_B, D])
        row = sb(g, ph, "row0", [P, 2, ROWS_B, D + 2])
        stat = sb(g, ph, "stat0", [P, 2, ROWS_B, 6])
        agg = sb(g, ph, "agg0", [P, 2, ROWS_B, 2])
        std = sb(g, ph, "std0", [P, 2, ROWS_B])
        rstd = sb(g, ph, "rstd0", [P, 2, ROWS_B])
        hT = sb(g, ph, "hT0", [P, 2, ROWS_B, P])
        th = sb(g, ph, "th0", [P, 2, ROWS_B, D])
        w1 = sb(g, ph, "w1", [P, D])
        zero_rows = sb(g, ph, "zero_rows", [P, 3 * ACC_W], BF16)
        w1T = sb(g, ph, "w1T", [P, D])
        w2b = sb(g, ph, "w2b", [P, D])
        ps_h = [pb(g, ph, f"ps_h0{k}", [P, 8 * P]) for k in range(2)]
        ps_z = [pb(g, ph, f"ps_z0{k}", [P, 8 * P]) for k in range(2)]
        block = ph.enter_context(nc.Block())

        @block.sync
        def _(sp):
            sp.dma_start(w1[:], t["L0_gnn_W1"]).then_inc(s_w, 16)
            sp.dma_start(w2b[:], t["L0_gnn_w2"].rearrange("(a n) -> a n", a=1).to_broadcast([P, D]))\
              .then_inc(s_w, 16)

            def step(n, u):
                if has(n, BATCHES):
                    D_["normal"].wait(sp, n - 2)
                    sp.dma_start(xb[:, u], rows_of(t["x"], n)).then_inc(d_in[u], 16)
                k, v = n - 1, (u - 1) % 2
                if has(k, BATCHES):
                    D_["weighed"].wait(sp, k)
                    sp.dma_start(rows_of(g.pool_rows, k), row[:, v]).then_inc(d_out[v], 16)
            sp.wait_ge(s_wdve, 1)
            for W in (D, ACC_W):
                sp.dma_start(g.parts[W][NODES:NODES + P, :], zero_rows[:, 0:3 * W]).then_inc(s_w, 16)
            rolled(sp, BATCHES, 2, 1, step)
            for v in range(2):
                sp.wait_ge(d_out[v], 16 * BATCHES // 2)
            sp.wait_ge(s_w, 64)

        @block.vector
        def _(dve):
            V.memset(zero_rows[:], 0.0)
            V.memset(row[:, :, :, D:D + 1], 1.0)
            V.memset(acc[:], 0.0)
            V.memset(run_max[:], -BIG)
            dve.wait_ge(s_wpe, 1)
            V.tensor_copy(w1T[:], ps_z[0][:, 0:D]).then_inc(s_wdve, 1)

            def step(n, u):
                if has(n, BATCHES):
                    dve.wait_ge(d_in[u], n * 8 + (16 - 8 * u))
                    for j in range(ROWS_B):
                        i = V.bn_stats(stat[:, u, j], xb[:, u, j])
                    i.then_inc(D_["stats"].sem, 1)
                    D_["stats"].wait(dve, n)
                    settle(g, dve)
                    for j in range(ROWS_B):
                        i = V.bn_aggr(agg[:, u, j], stat[:, u, j])
                    i.then_inc(D_["var"].sem, 1)
                    D_["std"].wait(dve, n)
                    V.reciprocal(rstd[:, u], std[:, u]).then_inc(D_["rstd"].sem, 1)
                    if not isinstance(n, int) or n >= 2:
                        dve.wait_ge(d_out[u], (n - 2) * 8 + (16 - 8 * u))
                    D_["rstd"].wait(dve, n)
                    for j in range(ROWS_B):
                        i = V.tensor_scalar(row[:, u, j, 0:D], xb[:, u, j], agg[:, u, j, 0:1],
                                            rstd[:, u, j:j + 1], ALU.subtract, ALU.mult)
                    i.then_inc(D_["normal"].sem, 1)
                    D_["normal"].wait(dve, n)
                    V.tensor_scalar(row[:, u, :, 0:D], row[:, u, :, 0:D], 0.0, None, ALU.max)\
                     .then_inc(D_["hidden"].sem, 1)
                k, v = n - 1, (u - 1) % 2
                if has(k, BATCHES):
                    D_["tanh"].wait(dve, k)
                    V.tensor_tensor(out=th[:, v], in0=th[:, v],
                                    in1=w2b[:].unsqueeze(1).to_broadcast([P, ROWS_B, D]), op=ALU.mult)\
                     .then_inc(D_["extra"].sem, 1)
                    D_["extra"].wait(dve, k)
                    V.tensor_reduce(row[:, v, :, D + 1:D + 2], th[:, v], AX.X, ALU.add)\
                     .then_inc(D_["weighed"].sem, 1)
            dve.wait_ge(s_w, 32)
            rolled(dve, BATCHES, 2, 1, step)

        @block.tensor
        def _(pe):
            pe.wait_ge(s_w, 32)
            T_.transpose(ps_z[0][:, 0:D], w1[:], ident[:]).then_inc(s_wpe, 1)
            pe.wait_ge(s_wdve, 1)

            def step(n, u):
                D_["hidden"].wait(pe, n)
                D_["turned_sb"].wait(pe, n - 2)
                for j in range(ROWS_B):
                    i = T_.transpose(ps_h[u][:, j * P:(j + 1) * P], row[:, u, j, 0:D], ident[:])
                i.then_inc(D_["turned"].sem, 1)
                D_["turned_sb"].wait(pe, n)
                D_["tanh"].wait(pe, n - 2)
                for j in range(ROWS_B):
                    i = T_.matmul(ps_z[u][:, j * P:(j + 1) * P], hT[:, u, j], w1T[:], start=True, stop=True)
                i.then_inc(D_["product"].sem, 1)
            rolled(pe, BATCHES, 2, 0, step)

        @block.scalar
        def _(act):
            def step(n, u):
                D_["var"].wait(act, n)
                S_.activation(std[:, u], agg[:, u, :, 1], ACT.Sqrt, bias=ln_eps[:]).then_inc(D_["std"].sem, 1)
                D_["turned"].wait(act, n)
                S_.activation(hT[:, u], ps_h[u][:, 0:ROWS_B * P].rearrange("p (j n) -> p j n", n=P), ACT.Copy)\
                  .then_inc(D_["turned_sb"].sem, 1)
                D_["product"].wait(act, n)
                D_["weighed"].wait(act, n - 2)
                S_.activation(th[:, u], ps_z[u][:, 0:ROWS_B * P].rearrange("p (j n) -> p j n", n=P), ACT.Tanh)\
                  .then_inc(D_["tanh"].sem, 1)
            rolled(act, BATCHES, 2, 0, step)
    bump(g, "stats", "var", "std", "rstd", "normal", "hidden", "turned", "turned_sb", "product", "tanh",
         "weighed", "extra")


class Items:

    def __init__(self, g, eng, lag=U):
        self.g, self.eng, self.lag = g, eng, lag

    def begin(self, r):
        self.known, self.words = {}, {}
        for w in range((U - self.lag) // PACK, 2 * U // PACK):
            at = r * (U // PACK) + (w - U // PACK)
            if not isinstance(at, int) or 0 <= at < GROUPS:
                self.words[w] = self.eng.value_load(self.g.item_words[0:1, ds(at, 1)])

    def _unpacked(self, k, tile):
        if (k, tile) not in self.known:
            word = self.words[k // PACK]
            if k % PACK == 0:
                value = (word >> 9) & 127 if tile else word & 511
            else:
                value = self._unpacked(k - 1, tile) + ((word >> (14 + 2 * (k % PACK) + tile)) & 1)
            self.known[k, tile] = self.g.nc.s_assert_within(
                self.eng.snap(value), 0, NODE_TILES if tile else BLOCKS - 1,
                skip_runtime_bounds_check_because="the item list was clamped to it on the chip")
        return self.known[k, tile]

    def block(self, u, lag=0):
        return self._unpacked(U + u - lag, 0)

    def tile(self, u, lag=0):
        return self._unpacked(U + u - lag, 1)


EDGE_SIGNALS = ("rel", "onehot", "kv", "prod", "alpha", "scan", "ends", "shown", "peak", "fresh_max",
                "drop", "kept_max", "gap", "message", "scaled", "summed",
                "onehotT", "query", "attrT", "edge", "alphaT", "prefix", "tile_max", "edge_max",
                "partial",
                "onehotT_sb", "attrT_sb", "onehot32", "rows", "absent", "factor", "weight")


def edge_signals(g):
    g.edge = {k: Signal(sem(g, "edge_" + k)) for k in EDGE_SIGNALS}
    g.resets_loaded = [sem(g, f"resets_loaded{k}") for k in range(U)]
    g.attrs_loaded = [sem(g, f"attrs_loaded{k}") for k in range(U)]
    g.query_loaded = [sem(g, f"query_loaded{k}") for k in range(QB)]
    g.resets_base = g.attrs_base = g.query_base = 0


def edge_stage(g, kind, rows, width, heads, ring_blocks):
    nc, t = g.nc, g.t
    V, S_, T_ = nc.vector, nc.scalar, nc.tensor
    E, H, R = g.edge, heads, ring_blocks
    pool_k, multi, single = kind == "pool", kind == "multi", kind == "single"
    acc_w = {"pool": D + 1, "multi": H * HW, "single": ACC_W}[kind]
    query_w = ACC_W if single else D
    gathered = [sem(g, f"{kind}_gathered{k}") for k in range(R)]
    index_ready = sem(g, f"{kind}_index_ready")
    blocks_ready = sem(g, f"{kind}_blocks_ready")
    ring_read = E["kv" if multi else "rows"]
    resets_base, attrs_base, query_base = g.resets_base, g.attrs_base, g.query_base

    with ExitStack() as ph:
        ring = sb(g, ph, f"ring_{kind}", [P, R, J, width])
        index = sb(g, ph, f"index_{kind}", [P, R, J], U32)
        rel = sb(g, ph, f"rel_{kind}", [P, U, J])
        onehot = sb(g, ph, f"onehot_{kind}", [P, U, J, P], BF16)
        onehotT = sb(g, ph, f"onehotT_{kind}", [P, U, J, P], BF16)
        reset = sb(g, ph, f"reset_{kind}", [J * H, U, P])
        prefix = sb(g, ph, f"prefix_{kind}", [J * H, 2, P])
        ends = sb(g, ph, f"ends_{kind}", [P, 2, J, H + 1], BF16)
        absent = sb(g, ph, f"absent_{kind}", [P, 2, J])
        shown = sb(g, ph, f"shown_{kind}", [P, 2, J, H])
        peak = sb(g, ph, f"peak_{kind}", [P, 2, H])
        fresh = sb(g, ph, f"fresh_{kind}", [P, 2, H], BF16)
        drop = sb(g, ph, f"drop_{kind}", [P, 2, H])
        factor = sb(g, ph, f"factor_{kind}", [P, 4, H])
        gap = sb(g, ph, f"gap_{kind}", [P, 2, J, H])
        if multi:
            kv = sb(g, ph, "kv", [P, 4, J, 2, D])
            prod = sb(g, ph, "prod_multi", [P, J, D])
            onehot32 = sb(g, ph, "onehot32", [P, 2, J, P])
            message = sb(g, ph, "message_multi", [P, 2, J, H, HW])
            attr = sb(g, ph, "attr_multi", [P, U, J, EDGE_DIM])
            attrT = sb(g, ph, "attrT", [J * EDGE_DIM, 2, P])
            w_edge = sb(g, ph, "w_edge", [J * EDGE_DIM, J, D])
        else:
            weight = sb(g, ph, f"weight_{kind}", [P, 2, J])
            message = sb(g, ph, f"message_{kind}", [P, 2, J, P])
            row = sb(g, ph, f"row_{kind}", [P, U, J, ACC_W if single else width])
        if single:
            prod = sb(g, ph, "prod_single", [P, J, ACC_W])
        if not pool_k:
            alpha = sb(g, ph, f"alpha_{kind}", [P, U, J * H])
            query = sb(g, ph, f"query_{kind}", [P, QB, 3, query_w], BF16)
        ps_s = pb(g, ph, f"ps_s_{kind}", [P, J * P])
        ps_q = pb(g, ph, f"ps_q_{kind}", [P, J, D])
        ps_e = pb(g, ph, f"ps_e_{kind}", [P, 512])
        ps_a = pb(g, ph, f"ps_a_{kind}", [P, 512])
        ps_f = pb(g, ph, f"ps_f_{kind}", [P, 512])
        ps_m = pb(g, ph, f"ps_m_{kind}", [P, 512])
        ps_x = pb(g, ph, f"ps_x_{kind}", [P, 512])
        ps_p = pb(g, ph, f"ps_p_{kind}", [P, 512])
        turned = ps_s[:, 0:J * P // 2].bitcast(BF16).rearrange("p (j n) -> p j n", j=J)
        tile_max = ps_m[:, 0:J * (H + 1)].rearrange("p (j h) -> p j h", j=J)
        edge_max = ps_x[:, 0:J * H].rearrange("p (j h) -> p j h", j=J)
        tail_q = ps_e[:, 0:J * TAIL].rearrange("p (j c) -> p j c", j=J)
        block = ph.enter_context(nc.Block())

        def logits(u):
            return row[:, u, :, D + 1] if pool_k else alpha[:, u]

        def in_ring(items, u, lag, a, b):
            slot = ds(items.block(u, lag) & (R - 1), 1)
            return ring[:, slot, :, a:b].rearrange("p r j w -> p (r j) w")

        @block.gpsimd
        def _(pool):
            def step(n, u):
                if has(n, BLOCKS):
                    nc.gpsimd.tensor_copy(index[:, u], g.src_cols[:, ds(n * J, J)]).then_inc(index_ready, 1)
                    if not isinstance(n, int) or n >= R:
                        items_done = pool.value_load(g.block_ends[0:1, ds(n - R, 1)], min_val=1, max_val=ITEMS)
                        pool.wait_ge(ring_read.sem, items_done + ring_read.base)
                    pool.wait_ge(index_ready, n + 1)
                    settle(g, pool)
                    for j in range(J):
                        pool.indirect_dma_start(
                            out=ring[:, u, j, :], out_offset=None, in_=rows,
                            in_offset=bass.IndirectOffsetOnAxis(ap=index[:, u, j:j + 1], axis=0),
                        ).then_inc(gathered[u], 16)
                k, v = n - 1, (u - 1) % R
                if has(k, BLOCKS):
                    pool.wait_ge(gathered[v], k * (16 * J // R) + (16 * J - v * (16 * J // R)))
                    pool.sem_inc(blocks_ready, 1)
            rolled(pool, BLOCKS, R, 1, step, peel=1)

        @block.sync
        def _(sp):
            if multi:
                sp.wait_ge(g.w_edge_clear, 1)
                for j in range(J):
                    sp.dma_start(w_edge[j * EDGE_DIM:(j + 1) * EDGE_DIM, j, :], t["L1_gnn_We0"])\
                      .then_inc(g.w_edge_loaded, 16)
            items = Items(g, sp, 0)

            def step(n, u):
                b = items.block(u)
                E["scan"].wait(sp, n - U)
                settle(g, sp)
                src = g.resets[ds(b * J, J), :]
                if H > 1:
                    src = src.unsqueeze(1).to_broadcast([J, H, P])
                sp.dma_start(reset[:, u], src).then_inc(g.resets_loaded[u], 16)
                if not pool_k:
                    E["query"].wait(sp, n - QB)
                    settle(g, sp)
                    sp.dma_start(query[:, u % QB].rearrange("p a c -> p (a c)"),
                                 g.parts[query_w].rearrange("(t p) c -> p t c", p=P)[:, ds(items.tile(u), 1), :]
                                 .rearrange("p t c -> p (t c)")).then_inc(g.query_loaded[u % QB], 16)
                    E["attrT" if multi else "partial"].wait(sp, n - U)
                    settle(g, sp)
                    sp.dma_start(attr[:, u] if multi else row[:, u, :, D:D + EDGE_DIM],
                                 t["edge_attr_16"].rearrange("(k p) c -> p k c", p=P)[:, ds(b * J, J), :])\
                      .then_inc(g.attrs_loaded[u], 16)
            rolled(sp, ITEMS, U, 0, step, items.begin, peel=1)

        def loaded(eng, sems, base, n, u):
            per = 16 // len(sems)
            eng.wait_ge(sems[u % len(sems)], n * per + (16 - (u % len(sems)) * per + base))

        @block.vector
        def _(dve):
            items = Items(g, dve, 5)
            if multi:
                V.memset(w_edge[:], 0.0).then_inc(g.w_edge_clear, 1)
            if single:
                V.memset(row[:, :, :, ACC_W - 1:ACC_W], 1.0)
            V.memset(g.run_max[:], -BIG)
            V.memset(g.acc[:], 0.0).then_inc(g.acc_clear, 1)
            dve.wait_ge(g.acc_clear, 1 + ("pool", "multi", "single").index(kind))

            def step(n, u):
                m1, u1 = n - 1, (u - 1) % U
                m2, u2, p2 = n - 2, (u - 2) % U, u % 2
                m3, u3, p3 = n - 3, (u - 3) % U, (u - 3) % 2
                m4, u4, p4 = n - 4, (u - 4) % U, u % 2
                m5, f5 = n - 5, (u - 5) % 4
                if has(n, ITEMS):
                    V.tensor_scalar(rel[:, u], g.dst_cols[:, ds(items.block(u) * J, J)],
                                    g.tile_base[:, ds(items.tile(u), 1)], None, ALU.subtract)\
                     .then_inc(E["rel"].sem, 1)
                if has(m5, ITEMS):
                    a5 = g.acc[:, ds(items.tile(u, 5), 1), 0:acc_w]
                if multi and has(m5, ITEMS):
                    E["factor"].wait(dve, m5)
                    E["summed"].wait(dve, m5 - 1)
                    a5h = a5.rearrange("p t (h c) -> p (t h) c", h=H)
                    V.tensor_tensor(out=a5h, in0=a5h, in1=factor[:, f5].unsqueeze(2).to_broadcast([P, H, HW]),
                                    op=ALU.mult).then_inc(E["scaled"].sem, 1)
                if has(m3, ITEMS):
                    E["tile_max"].wait(dve, m3)
                    E["absent"].wait(dve, m3)
                    V.tensor_tensor(out=shown[:, p3], in0=tile_max[:, :, 0:H],
                                    in1=absent[:, p3].unsqueeze(2).to_broadcast([P, J, H]), op=ALU.add)\
                     .then_inc(E["shown"].sem, 1)
                if has(m2, ITEMS):
                    E["alphaT"].wait(dve, m2)
                    E["prefix"].wait(dve, m2 - 2)
                    loaded(dve, g.resets_loaded, resets_base, m2, u2)
                    V.tensor_tensor_scan(prefix[:, p2], reset[:, u2], ps_a[0:J * H, 0:P], -BIG, ALU.add, ALU.max)\
                     .then_inc(E["scan"].sem, 1)
                if has(n, ITEMS):
                    E["rel"].wait(dve, n)
                    E["partial"].wait(dve, n - U)
                    for j in range(J):
                        i = V.tensor_scalar(onehot[:, u, j], g.iota_b[:], rel[:, u, j:j + 1], None, ALU.is_equal)
                    i.then_inc(E["onehot"].sem, 1)
                if has(m3, ITEMS):
                    E["shown"].wait(dve, m3)
                    V.tensor_reduce(peak[:, p3], shown[:, p3].rearrange("p j h -> p h j"), AX.X, ALU.max)\
                     .then_inc(E["peak"].sem, 1)
                if multi and has(m1, ITEMS):
                    E["edge"].wait(dve, m1)
                    E["message"].wait(dve, m1 - 4)
                    dve.wait_ge(blocks_ready, items.block(u, 1) + 1)
                    V.tensor_tensor(out=kv[:, u1 % 4],
                                    in0=in_ring(items, u, 1, 0, 2 * D).rearrange("p j (a c) -> p j a c", a=2),
                                    in1=ps_e[:].rearrange("p (j c) -> p j c", j=J).unsqueeze(2)
                                    .to_broadcast([P, J, 2, D]), op=ALU.add).then_inc(E["kv"].sem, 1)
                if has(m3, ITEMS):
                    kept = g.run_max[:, ds(items.tile(u, 3), 1), 0:H].rearrange("p t h -> p (t h)")
                    E["peak"].wait(dve, m3)
                    E["kept_max"].wait(dve, m3 - 1)
                    E["edge_max"].wait(dve, m3 - 2)
                    V.tensor_tensor(out=fresh[:, p3], in0=peak[:, p3], in1=kept, op=ALU.max)\
                     .then_inc(E["fresh_max"].sem, 1)
                if has(m4, ITEMS):
                    E["weight"].wait(dve, m4)
                    E["partial"].wait(dve, m4 - 2)
                    if multi:
                        i = V.tensor_tensor(
                            out=message[:, p4, :, :, 0:HEAD_DIM],
                            in0=kv[:, u4 % 4, :, 1, :].rearrange("p j (h c) -> p j h c", h=H),
                            in1=message[:, p4, :, :, HEAD_DIM:HW].to_broadcast([P, J, H, HEAD_DIM]), op=ALU.mult)
                    else:
                        for j in range(J):
                            i = V.tensor_scalar(message[:, p4, j], onehot[:, u4, j], weight[:, p4, j:j + 1], None,
                                                ALU.mult)
                    i.then_inc(E["message"].sem, 1)
                if has(m3, ITEMS):
                    E["fresh_max"].wait(dve, m3)
                    E["factor"].wait(dve, m3 - 2)
                    V.tensor_tensor(out=drop[:, p3], in0=kept, in1=fresh[:, p3], op=ALU.subtract)\
                     .then_inc(E["drop"].sem, 1)
                if has(m5, ITEMS):
                    a5 = a5.rearrange("p t c -> p (t c)")
                    E["partial"].wait(dve, m5)
                    if multi:
                        E["scaled"].wait(dve, m5)
                        i = V.tensor_tensor(out=a5, in0=a5, in1=ps_p[:, 0:acc_w], op=ALU.add)
                    else:
                        E["factor"].wait(dve, m5)
                        E["summed"].wait(dve, m5 - 1)
                        i = V.scalar_tensor_tensor(out=a5, in0=a5, scalar=factor[:, f5, 0:1],
                                                   in1=ps_p[:, 0:acc_w], op0=ALU.mult, op1=ALU.add)
                    i.then_inc(E["summed"].sem, 1)
                if has(m1, ITEMS) and not pool_k:
                    E["query"].wait(dve, m1)
                    E["alpha"].wait(dve, m1 - 1)
                    if multi:
                        E["kv"].wait(dve, m1)
                        i = V.tensor_tensor(out=prod[:], in0=kv[:, u1 % 4, :, 0, :], in1=ps_q[:], op=ALU.mult)
                    else:
                        E["rows"].wait(dve, m1)
                        loaded(dve, g.attrs_loaded, attrs_base, m1, u1)
                        V.tensor_tensor(out=prod[:, :, 0:D], in0=row[:, u1, :, 0:D], in1=ps_q[:], op=ALU.mult)
                        i = V.tensor_tensor(out=prod[:, :, D:ACC_W], in0=row[:, u1, :, D:ACC_W], in1=tail_q,
                                            op=ALU.mult)
                    i.then_inc(E["prod"].sem, 1)
                if has(m2, ITEMS):
                    last = g.last_cols[:, ds(items.block(u, 2) * J, J)].unsqueeze(2)
                    E["prefix"].wait(dve, m2)
                    E["tile_max"].wait(dve, m2 - 2)
                    V.tensor_scalar(ends[:, p2, :, H:H + 1], last, BIG, None, ALU.mult)
                    V.tensor_tensor(out=ends[:, p2, :, 0:H],
                                    in0=ps_f[:, 0:J * H].rearrange("p (j h) -> p j h", j=J),
                                    in1=last.to_broadcast([P, J, H]), op=ALU.mult).then_inc(E["ends"].sem, 1)
                if has(m1, ITEMS) and not pool_k:
                    E["prod"].wait(dve, m1)
                    V.tensor_reduce(alpha[:, u1], prod[:].rearrange("p j (h c) -> p (j h) c", h=H), AX.X, ALU.add)\
                     .then_inc(E["alpha"].sem, 1)
                if has(m3, ITEMS):
                    E["edge_max"].wait(dve, m3)
                    E["weight"].wait(dve, m3 - 2)
                    V.tensor_tensor(out=gap[:, p3], in0=logits(u3).rearrange("p (j h) -> p j h", j=J),
                                    in1=edge_max, op=ALU.subtract).then_inc(E["gap"].sem, 1)
                    E["drop"].wait(dve, m3)
                    settle(g, dve)
                    V.tensor_copy(kept, fresh[:, p3]).then_inc(E["kept_max"].sem, 1)
            rolled(dve, ITEMS, U, 5, step, items.begin, peel=1)

        @block.tensor
        def _(pe):
            if multi:
                pe.wait_ge(g.w_edge_loaded, 16 * J)

            def step(n, u):
                m2, u2, p2 = n - 2, (u - 2) % U, u % 2
                m3, u3, p3 = n - 3, (u - 3) % U, (u - 3) % 2
                m5, u5, p5 = n - 5, (u - 5) % U, (u - 5) % 2
                if multi and has(n, ITEMS):
                    loaded(pe, g.attrs_loaded, attrs_base, n, u)
                    E["onehotT_sb"].wait(pe, n - 1)
                    settle(g, pe)
                    T_.transpose(ps_s[0:J * EDGE_DIM, 0:P], attr[:, u].rearrange("p j c -> p (j c)"),
                                 g.ident[:]).then_inc(E["attrT"].sem, 1)
                if has(m2, ITEMS):
                    E["rows" if pool_k else "alpha"].wait(pe, m2)
                    E["scan"].wait(pe, m2 - 1)
                    settle(g, pe)
                    T_.transpose(ps_a[0:J * H, 0:P], logits(u2), g.ident[:]).then_inc(E["alphaT"].sem, 1)
                if has(m5, ITEMS):
                    E["message"].wait(pe, m5)
                    E["summed"].wait(pe, m5 - 1)
                    if multi:
                        E["onehot32"].wait(pe, m5)
                    for j in range(J):
                        if multi:
                            lhs, rhs = onehot32[:, p5, j], message[:, p5, j].rearrange("p h c -> p (h c)")
                        else:
                            lhs = message[:, p5, j]
                            rhs = row[:, u5, j, 0:acc_w]
                        i = T_.matmul(ps_p[:, 0:acc_w], lhs, rhs, start=(j == 0), stop=(j == J - 1))
                    i.then_inc(E["partial"].sem, 1)
                if has(n, ITEMS):
                    E["onehot"].wait(pe, n)
                    E["attrT_sb" if multi else "onehotT_sb"].wait(pe, n if multi else n - 1)
                    for j in range(J):
                        i = T_.transpose(turned[:, j], onehot[:, u, j], g.ident_b[:])
                    i.then_inc(E["onehotT"].sem, 1)
                if has(m2, ITEMS):
                    E["scan"].wait(pe, m2)
                    E["ends"].wait(pe, m2 - 1)
                    settle(g, pe)
                    T_.transpose(ps_f[:, 0:J * H], prefix[:, p2], g.ident[0:J * H, 0:J * H])\
                      .then_inc(E["prefix"].sem, 1)
                if multi and has(n, ITEMS):
                    E["attrT_sb"].wait(pe, n)
                    E["kv"].wait(pe, n - 1)
                    T_.matmul(ps_e[:], attrT[:, u % 2], w_edge[:].rearrange("k j c -> k (j c)"),
                              start=True, stop=True).then_inc(E["edge"].sem, 1)
                if has(m3, ITEMS):
                    E["fresh_max"].wait(pe, m3)
                    E["onehotT_sb"].wait(pe, m3)
                    E["gap"].wait(pe, m3 - 1)
                    for j in range(J):
                        i = T_.matmul(edge_max[:, j], onehotT[:, u3, j], fresh[:, p3], start=True, stop=True)
                    i.then_inc(E["edge_max"].sem, 1)
                if has(m2, ITEMS):
                    E["ends"].wait(pe, m2)
                    E["shown"].wait(pe, m2 - 1)
                    E["absent"].wait(pe, m2 - 1)
                    for j in range(J):
                        i = T_.matmul(tile_max[:, j], onehot[:, u2, j], ends[:, p2, j], start=True, stop=True)
                    i.then_inc(E["tile_max"].sem, 1)
                if not pool_k and has(n, ITEMS):
                    loaded(pe, g.query_loaded, query_base, n, u)
                    E["onehotT_sb"].wait(pe, n)
                    E["prod"].wait(pe, n - 1)
                    for j in range(J):
                        for k in range(3):
                            i = T_.matmul(ps_q[:, j], onehotT[:, u, j], query[:, u % QB, k, 0:D],
                                          start=(k == 0), stop=(k == 2))
                        for k in range(3 if single else 0):
                            i = T_.matmul(tail_q[:, j], onehotT[:, u, j], query[:, u % QB, k, D:ACC_W],
                                          start=(k == 0), stop=(k == 2))
                    i.then_inc(E["query"].sem, 1)
            rolled(pe, ITEMS, U, 5, step, peel=1)

        @block.scalar
        def _(act):
            items = Items(g, act, 0)
            copied = D if single else width

            def step(n, u):
                m2, p2 = n - 2, u % 2
                m3, u3, p3, f3 = n - 3, (u - 3) % U, (u - 3) % 2, (u - 3) % 4
                if multi and has(n, ITEMS):
                    E["attrT"].wait(act, n)
                    E["edge"].wait(act, n - 2)
                    S_.activation(attrT[:, u % 2], ps_s[0:J * EDGE_DIM, 0:P], ACT.Copy)\
                      .then_inc(E["attrT_sb"].sem, 1)
                if has(n, ITEMS):
                    E["onehotT"].wait(act, n)
                    E["edge_max"].wait(act, n - U)
                    S_.activation(onehotT[:, u], turned, ACT.Copy).then_inc(E["onehotT_sb"].sem, 1)
                if multi and has(m3, ITEMS):
                    E["partial"].wait(act, m3 - 2)
                    S_.activation(onehot32[:, p3], onehot[:, u3], ACT.Copy).then_inc(E["onehot32"].sem, 1)
                if has(m2, ITEMS):
                    E["tile_max"].wait(act, m2)
                    E["shown"].wait(act, m2 - 2)
                    S_.activation(absent[:, p2], tile_max[:, :, H], ACT.Identity, bias=g.neg_big[:])\
                      .then_inc(E["absent"].sem, 1)
                if not multi and has(n, ITEMS):
                    E["partial"].wait(act, n - U)
                    act.wait_ge(blocks_ready, items.block(u) + 1)
                    settle(g, act)
                    S_.activation(row[:, u, :, 0:copied], in_ring(items, u, 0, 0, copied), ACT.Copy)\
                      .then_inc(E["rows"].sem, 1)
                if has(m3, ITEMS):
                    E["drop"].wait(act, m3)
                    E["summed"].wait(act, m3 - 4)
                    S_.activation(factor[:, f3], drop[:, p3], ACT.Exp).then_inc(E["factor"].sem, 1)
                    E["gap"].wait(act, m3)
                    if multi:
                        E["partial"].wait(act, m3 - 2)
                        i = S_.activation(message[:, p3, :, :, HEAD_DIM:HW].rearrange("p j h c -> p j (h c)"),
                                          gap[:, p3], ACT.Exp)
                    else:
                        E["message"].wait(act, m3 - 2)
                        i = S_.activation(weight[:, p3].unsqueeze(2), gap[:, p3], ACT.Exp)
                    i.then_inc(E["weight"].sem, 1)
            rolled(act, ITEMS, U, 3, step, None if multi else items.begin, peel=1)

    for k in EDGE_SIGNALS:
        used = {"kv": multi, "attrT": multi, "edge": multi, "attrT_sb": multi, "scaled": multi,
                "prod": not pool_k, "alpha": not pool_k, "query": not pool_k, "onehot32": multi, "rows": not multi}.get(k, True)
        E[k].base += ITEMS if used else 0
    g.resets_base += ITEMS * 16 // U
    g.attrs_base += 0 if pool_k else ITEMS * 16 // U
    g.query_base += 0 if pool_k else ITEMS * 16 // QB



def waits_of_buffer(eng, sems, base, n, u):
    eng.wait_ge(sems[u], n * 8 + (16 - 8 * u + base))


def norm_front(g, dve, n, u, x, stat, agg, std, rstd, out, free):
    V, D_ = g.nc.vector, g.dense
    for j in range(ROWS_B):
        i = V.bn_stats(stat[:, u, j], x[:, u, j])
    i.then_inc(D_["stats"].sem, 1)
    D_["stats"].wait(dve, n)
    settle(g, dve)
    for j in range(ROWS_B):
        i = V.bn_aggr(agg[:, u, j], stat[:, u, j])
    i.then_inc(D_["var"].sem, 1)
    D_["std"].wait(dve, n)
    V.reciprocal(rstd[:, u], std[:, u]).then_inc(D_["rstd"].sem, 1)
    free()
    D_["rstd"].wait(dve, n)
    for j in range(ROWS_B):
        i = V.tensor_scalar(out[:, u, j, 0:D], x[:, u, j], agg[:, u, j, 0:1], rstd[:, u, j:j + 1],
                            ALU.subtract, ALU.mult)
    i.then_inc(D_["normal"].sem, 1)
    D_["normal"].wait(dve, n)
    V.tensor_scalar(out[:, u, :, 0:D], out[:, u, :, 0:D], 0.0, None, ALU.max).then_inc(D_["hidden"].sem, 1)


def split(g, dve, n, x, parts):
    V, D_ = g.nc.vector, g.dense
    part, rest = D_["part"], D_["rest"]
    V.tensor_copy(parts[:, :, 0], x).then_inc(part.sem, 1)
    for k in range(2):
        part.wait(dve, n * 2 + k)
        V.tensor_tensor(out=x, in0=x, in1=parts[:, :, k], op=ALU.subtract).then_inc(rest.sem, 1)
        rest.wait(dve, n * 2 + k)
        V.tensor_copy(parts[:, :, k + 1], x).then_inc((part if k == 0 else D_["query_done"]).sem, 1)


def bump(g, *used, per_tile=()):
    for k in used:
        g.dense[k].base += BATCHES * (ROWS_B if k in per_tile else 2 if k in ("part", "rest") else 1)


def row_of(vector, n=D):
    return vector.rearrange("(a n) -> a n", a=1)


def project_stage(g):
    nc, t, ident, acc = g.nc, g.t, g.ident, g.acc
    V, S_, T_ = nc.vector, nc.scalar, nc.tensor
    D_ = g.dense
    loaded = [sem(g, f"x_loaded{k}") for k in range(2)]
    stored = [sem(g, f"kv_stored{k}") for k in range(2)]
    s_w, s_wdve = sem(g, "project_weights_loaded"), sem(g, "project_weights_ready")
    evac = D_["product_read"]
    with ExitStack() as ph:
        xb = sb(g, ph, "xb1", [P, 2, ROWS_B, D])
        pooled = sb(g, ph, "pooled", [P, ROWS_B, D])
        den = sb(g, ph, "den1", [P, 2, ROWS_B])
        stat = sb(g, ph, "stat1", [P, 2, ROWS_B, 6])
        agg = sb(g, ph, "agg1", [P, 2, ROWS_B, 2])
        std = sb(g, ph, "std1", [P, 2, ROWS_B])
        rstd = sb(g, ph, "rstd1", [P, 2, ROWS_B])
        h = sb(g, ph, "h1", [P, 2, ROWS_B, D])
        hT = sb(g, ph, "hT1", [P, ROWS_B, P])
        out = sb(g, ph, "out1", [P, 2, ROWS_B, 4 * D])
        parts = sb(g, ph, "parts1", [P, 2, ROWS_B, 3, D], BF16)
        w = sb(g, ph, "w_qkvs", [P, 4, D])
        bias = sb(g, ph, "b_qkvs", [P, 4, D])
        ps_h = pb(g, ph, "ps_h1", [P, 8, P])
        ps_z = [pb(g, ph, f"ps_z1{k}", [P, 512]) for k in range(4)]
        block = ph.enter_context(nc.Block())

        @block.sync
        def _(sp):
            for k, name in enumerate(("q", "k", "v", "s")):
                sp.dma_start(w[:, k], t[f"L1_gnn_W{name}0"]).then_inc(s_w, 16)
                sp.dma_start(bias[:, k], row_of(t[f"L1_gnn_b{name}0"]).to_broadcast([P, D])).then_inc(s_w, 16)

            def step(n, u):
                if has(n, BATCHES):
                    D_["normal"].wait(sp, n - 2)
                    if not isinstance(n, int) or n >= 2:
                        waits_of_stores(sp, n - 2, u)
                    sp.dma_start(xb[:, u], rows_of(t["x"], n)).then_inc(loaded[u], 16)
                k, v = n - 1, (u - 1) % 2
                if has(k, BATCHES):
                    D_["x_sum"].wait(sp, k)
                    sp.dma_start(rows_of(g.x1_rows, k), xb[:, v]).then_inc(stored[v], 16)
                    evac.wait(sp, k * ROWS_B + (ROWS_B - 1))
                    sp.dma_start(rows_of(g.kv_rows, k), out[:, v, :, D:3 * D]).then_inc(stored[v], 16)
                    sp.dma_start(rows_of(g.skip1_rows, k), out[:, v, :, 3 * D:4 * D]).then_inc(stored[v], 16)
                    D_["query_done"].wait(sp, k)
                    sp.dma_start(rows_of(g.parts[D][0:NODES], k),
                                 parts[:, v].rearrange("p t a c -> p t (a c)")).then_inc(stored[v], 16)

            def waits_of_stores(eng, n, u):
                eng.wait_ge(stored[u], n * 32 + (64 - 32 * u))
            rolled(sp, BATCHES, 2, 1, step)
            for v in range(2):
                sp.wait_ge(stored[v], 64 * BATCHES // 2)

        @block.vector
        def _(dve):
            dve.wait_ge(s_w, 128)
            V.tensor_scalar(w[:, 0], w[:, 0], HEAD_DIM ** -0.5, None, ALU.mult)
            V.tensor_scalar(bias[:, 0], bias[:, 0], HEAD_DIM ** -0.5, None, ALU.mult).then_inc(s_wdve, 1)
            dve.wait_ge(s_wdve, 1)

            def step(n, u):
                if has(n, BATCHES):
                    waits_of_buffer(dve, loaded, 0, n, u)
                    sums = acc[:, ds(n * ROWS_B, ROWS_B), :]
                    V.tensor_scalar(den[:, u].unsqueeze(2), sums[:, :, D:D + 1], 1e-30, None, ALU.max)\
                     .then_inc(D_["den"].sem, 1)
                    D_["den"].wait(dve, n)
                    V.reciprocal(den[:, u], den[:, u]).then_inc(D_["extra"].sem, 1)
                    D_["extra"].wait(dve, n)
                    V.tensor_tensor(out=pooled[:], in0=sums[:, :, 0:D],
                                    in1=den[:, u].unsqueeze(2).to_broadcast([P, ROWS_B, D]), op=ALU.mult)\
                     .then_inc(D_["acc_read"].sem, 1)
                    D_["acc_read"].wait(dve, n)
                    V.tensor_tensor(out=xb[:, u], in0=xb[:, u], in1=pooled[:], op=ALU.add)\
                     .then_inc(D_["x_sum"].sem, 1)
                    D_["x_sum"].wait(dve, n)
                    norm_front(g, dve, n, u, xb, stat, agg, std, rstd, h,
                               lambda: D_["turned"].wait(dve, n - 2))
                k, v = n - 1, (u - 1) % 2
                if has(k, BATCHES):
                    if not isinstance(k, int) or k >= 2:
                        dve.wait_ge(stored[v], (k - 2) * 32 + (64 - 32 * v))
                    for j in range(ROWS_B):
                        D_["product"].wait(dve, k * ROWS_B + j)
                        V.tensor_tensor(out=out[:, v, j], in0=ps_z[j % 4][:],
                                        in1=bias[:].rearrange("p a n -> p (a n)"), op=ALU.add)\
                         .then_inc(evac.sem, 1)
                    evac.wait(dve, k * ROWS_B + (ROWS_B - 1))
                    split(g, dve, k, out[:, v, :, 0:D], parts[:, v])
            rolled(dve, BATCHES, 2, 1, step)

        @block.tensor
        def _(pe):
            pe.wait_ge(s_wdve, 1)

            def step(n, u):
                D_["hidden"].wait(pe, n)
                D_["turned_sb"].wait(pe, n - 1)
                for j in range(ROWS_B):
                    i = T_.transpose(ps_h[:, j], h[:, u, j], ident[:])
                i.then_inc(D_["turned"].sem, 1)
                D_["turned_sb"].wait(pe, n)
                for j in range(ROWS_B):
                    evac.wait(pe, n * ROWS_B + (j - 3))
                    T_.matmul(ps_z[j % 4][:], hT[:, j], w[:].rearrange("p a n -> p (a n)"),
                              start=True, stop=True).then_inc(D_["product"].sem, 1)
            rolled(pe, BATCHES, 2, 0, step)

        @block.scalar
        def _(act):
            def step(n, u):
                if has(n, BATCHES):
                    D_["var"].wait(act, n)
                    S_.activation(std[:, u], agg[:, u, :, 1], ACT.Sqrt, bias=g.ln_eps[:])\
                      .then_inc(D_["std"].sem, 1)
                    D_["turned"].wait(act, n)
                    D_["product"].wait(act, n * ROWS_B - 1)
                    S_.activation(hT[:], ps_h[:, 0:ROWS_B], ACT.Copy).then_inc(D_["turned_sb"].sem, 1)
            rolled(act, BATCHES, 2, 0, step)
    bump(g, "acc_read", "x_sum", "stats", "var", "std", "rstd", "normal", "hidden", "turned", "turned_sb",
         "product", "product_read", "query_done", "part", "rest", "den", "extra", per_tile=("product", "product_read"))


def fold_stage(g):
    nc, t, ident, acc = g.nc, g.t, g.ident, g.acc
    V, S_, T_ = nc.vector, nc.scalar, nc.tensor
    D_ = g.dense
    loaded = [sem(g, f"skip_loaded{k}") for k in range(2)]
    stored = [sem(g, f"h2_stored{k}") for k in range(2)]
    s_w, s_wpe, s_wdve = sem(g, "fold_loaded"), sem(g, "fold_turned"), sem(g, "fold_ready")
    evac = D_["product_read"]
    with ExitStack() as ph:
        skip = sb(g, ph, "skip2", [P, 2, ROWS_B, D])
        x1 = sb(g, ph, "x12", [P, 2, ROWS_B, D])
        den = sb(g, ph, "den2", [P, 2, ROWS_B, HEADS])
        h = sb(g, ph, "h2", [P, 2, ROWS_B, D])
        hT = sb(g, ph, "hT2", [P, ROWS_B, P])
        qf = sb(g, ph, "qf", [P, ROWS_B, ACC_W])
        parts = sb(g, ph, "parts2", [P, 2, ROWS_B, 3, ACC_W], BF16)
        qT = sb(g, ph, "qT2", [P, ROWS_B, P])
        wq = sb(g, ph, "wq2", [P, D])
        ws = sb(g, ph, "ws2", [P, D])
        wk = sb(g, ph, "wk2", [P, D])
        we = sb(g, ph, "we2", [EDGE_DIM, D])
        bq = sb(g, ph, "bq2", [P, 1])
        bs = sb(g, ph, "bs2", [P, D])
        folded = sb(g, ph, "folded", [P, ACC_W])
        ps_h = pb(g, ph, "ps_h2", [P, 8, P])
        ps_q = pb(g, ph, "ps_q2", [P, 8, P])
        ps_z = [pb(g, ph, f"ps_z2{k}", [P, 512]) for k in range(4)]
        block = ph.enter_context(nc.Block())

        @block.sync
        def _(sp):
            for dest, src in ((wq[:], t["L1_gnn_Wq1"]), (ws[:], t["L1_gnn_Ws1"]), (wk[:], t["L1_gnn_Wk1"]),
                              (we[:], t["L1_gnn_We1"]), (bs[:], row_of(t["L1_gnn_bs1"]).to_broadcast([P, D])),
                              (bq[:], t["L1_gnn_bq1"].rearrange("(n a) -> n a", a=1)),
                              (folded[:, ACC_W - 1:ACC_W], t["L1_gnn_bk1"].rearrange("(n a) -> n a", a=1))):
                sp.dma_start(dest, src).then_inc(s_w, 16)

            def step(n, u):
                if has(n, BATCHES):
                    evac.wait(sp, (n - 2) * ROWS_B + (ROWS_B - 1))
                    if not isinstance(n, int) or n >= 2:
                        sp.wait_ge(stored[u], (n - 2) * 24 + (48 - 24 * u))
                    sp.dma_start(skip[:, u], rows_of(g.skip1_rows, n)).then_inc(loaded[u], 16)
                    sp.dma_start(x1[:, u], rows_of(g.x1_rows, n)).then_inc(loaded[u], 16)
                k, v = n - 1, (u - 1) % 2
                if has(k, BATCHES):
                    D_["hidden"].wait(sp, k)
                    sp.dma_start(rows_of(g.h2_rows, k), h[:, v]).then_inc(stored[v], 16)
                    evac.wait(sp, k * ROWS_B + (ROWS_B - 1))
                    sp.dma_start(rows_of(g.skip2_rows, k), x1[:, v]).then_inc(stored[v], 16)
                    D_["query_done"].wait(sp, k)
                    sp.dma_start(rows_of(g.parts[ACC_W][0:NODES], k),
                                 parts[:, v].rearrange("p t a c -> p t (a c)")).then_inc(stored[v], 16)
            rolled(sp, BATCHES, 2, 1, step)
            for v in range(2):
                sp.wait_ge(stored[v], 48 * BATCHES // 2)

        @block.vector
        def _(dve):
            dve.wait_ge(s_wpe, 1)
            V.tensor_copy(folded[:, 0:D + EDGE_DIM], ps_z[0][:, 0:D + EDGE_DIM])
            V.tensor_scalar(bq[:], bq[:], D ** -0.5, None, ALU.mult).then_inc(s_wdve, 1)

            def step(n, u):
                if has(n, BATCHES):
                    dve.wait_ge(loaded[u], n * 16 + (32 - 16 * u))
                    sums = acc[:, ds(n * ROWS_B, ROWS_B), 0:HEADS * HW]\
                        .rearrange("p t (h c) -> p t h c", h=HEADS)
                    V.tensor_scalar(den[:, u], sums[:, :, :, HEAD_DIM], DEN_EPS, None, ALU.add).then_inc(D_["den"].sem, 1)
                    D_["den"].wait(dve, n)
                    V.reciprocal(den[:, u], den[:, u]).then_inc(D_["extra"].sem, 1)
                    if not isinstance(n, int) or n >= 2:
                        dve.wait_ge(stored[u], (n - 2) * 24 + (48 - 24 * u))
                    D_["turned"].wait(dve, n - 2)
                    D_["extra"].wait(dve, n)
                    V.tensor_tensor(out=h[:, u].rearrange("p t (h c) -> p t h c", h=HEADS),
                                    in0=sums[:, :, :, 0:HEAD_DIM],
                                    in1=den[:, u].unsqueeze(3).to_broadcast([P, ROWS_B, HEADS, HEAD_DIM]),
                                    op=ALU.mult)\
                     .then_inc(D_["acc_read"].sem, 1)
                    D_["acc_read"].wait(dve, n)
                    V.tensor_tensor(out=h[:, u], in0=h[:, u], in1=skip[:, u], op=ALU.add)\
                     .then_inc(D_["x_sum"].sem, 1)
                    D_["x_sum"].wait(dve, n)
                    V.tensor_scalar(h[:, u], h[:, u], 0.0, None, ALU.max).then_inc(D_["hidden"].sem, 1)
                    V.tensor_tensor(out=x1[:, u], in0=x1[:, u],
                                    in1=bs[:].unsqueeze(1).to_broadcast([P, ROWS_B, D]), op=ALU.add)\
                     .then_inc(D_["weighed"].sem, 1)
                k, v = n - 1, (u - 1) % 2
                if has(k, BATCHES):
                    D_["weighed"].wait(dve, k)
                    D_["query_done"].wait(dve, k - 1)
                    for j in range(ROWS_B):
                        D_["product"].wait(dve, k * ROWS_B + j)
                        V.tensor_tensor(out=x1[:, v, j], in0=x1[:, v, j], in1=ps_z[j % 4][:, 0:D], op=ALU.add)
                        V.tensor_copy(qf[:, j], ps_z[j % 4][:, D:D + ACC_W]).then_inc(evac.sem, 1)
                    evac.wait(dve, k * ROWS_B + (ROWS_B - 1))
                    split(g, dve, k, qf[:], parts[:, v])
            rolled(dve, BATCHES, 2, 1, step)

        @block.tensor
        def _(pe):
            pe.wait_ge(s_w, 112)
            T_.transpose(ps_z[0][:, 0:D], wk[:], ident[:])
            T_.transpose(ps_z[0][:, D:D + EDGE_DIM], we[:], ident[0:EDGE_DIM, 0:EDGE_DIM]).then_inc(s_wpe, 1)
            pe.wait_ge(s_wdve, 1)

            def step(n, u):
                D_["hidden"].wait(pe, n)
                D_["turned_sb"].wait(pe, n - 1)
                for j in range(ROWS_B):
                    i = T_.transpose(ps_h[:, j], h[:, u, j], ident[:])
                i.then_inc(D_["turned"].sem, 1)
                D_["turned_sb"].wait(pe, n)
                D_["q_turned_sb"].wait(pe, n - 1)
                T_.matmul(ps_q[:, 0:4].rearrange("p j n -> p (j n)"), wq[:],
                          hT[:, 0:4].rearrange("p j n -> p (j n)"), start=True, stop=True)
                T_.matmul(ps_q[:, 4:ROWS_B].rearrange("p j n -> p (j n)"), wq[:],
                          hT[:, 4:ROWS_B].rearrange("p j n -> p (j n)"), start=True, stop=True)\
                  .then_inc(D_["q_turned"].sem, 1)
                D_["q_turned_sb"].wait(pe, n)
                for j in range(ROWS_B):
                    evac.wait(pe, n * ROWS_B + (j - 3))
                    T_.matmul(ps_z[j % 4][:, 0:D], hT[:, j], ws[:], start=True, stop=True)
                    T_.matmul(ps_z[j % 4][:, D:D + ACC_W], qT[:, j], folded[:], start=True, stop=True)\
                      .then_inc(D_["product"].sem, 1)
            rolled(pe, BATCHES, 2, 0, step)

        @block.scalar
        def _(act):
            act.wait_ge(s_wdve, 1)

            def step(n, u):
                D_["turned"].wait(act, n)
                D_["product"].wait(act, n * ROWS_B - 1)
                S_.activation(hT[:], ps_h[:, 0:ROWS_B], ACT.Copy).then_inc(D_["turned_sb"].sem, 1)
                D_["q_turned"].wait(act, n)
                S_.activation(qT[:], ps_q[:, 0:ROWS_B], ACT.Identity, bias=bq[:], scale=D ** -0.5)\
                  .then_inc(D_["q_turned_sb"].sem, 1)
            rolled(act, BATCHES, 2, 0, step)
    bump(g, "acc_read", "x_sum", "hidden", "turned", "turned_sb", "q_turned", "q_turned_sb", "weighed",
         "product", "product_read", "query_done", "part", "rest", "den", "extra", per_tile=("product", "product_read"))


def output_stage(g):
    nc, t, ident, acc = g.nc, g.t, g.ident, g.acc
    V, S_, T_ = nc.vector, nc.scalar, nc.tensor
    D_ = g.dense
    loaded = [sem(g, f"rest_loaded{k}") for k in range(2)]
    stored = [sem(g, f"out_stored{k}") for k in range(2)]
    s_w = sem(g, "output_weights_loaded")
    evac = D_["product_read"]
    with ExitStack() as ph:
        rest = sb(g, ph, "rest", [P, 2, ROWS_B, D])
        sums = sb(g, ph, "sums", [P, 2, ROWS_B, ACC_W])
        den = sb(g, ph, "den3", [P, 2, ROWS_B])
        sT = sb(g, ph, "sT", [P, ROWS_B, P])
        tT = sb(g, ph, "tT", [TAIL, ROWS_B, P])
        wv = sb(g, ph, "wv", [P, D])
        wt = sb(g, ph, "wt", [TAIL, D])
        ps_h = pb(g, ph, "ps_h3", [P, 8, P])
        ps_t = pb(g, ph, "ps_tail", [P, 8, P])
        ps_z = [pb(g, ph, f"ps_z3{k}", [P, 512]) for k in range(4)]
        block = ph.enter_context(nc.Block())

        @block.sync
        def _(sp):
            sp.dma_start(wv[:], t["L1_gnn_Wv1"]).then_inc(s_w, 16)
            sp.dma_start(wt[0:EDGE_DIM, :], t["L1_gnn_We1"]).then_inc(s_w, 16)
            sp.dma_start(wt[EDGE_DIM:TAIL, :], row_of(t["L1_gnn_bv1"])).then_inc(s_w, 16)

            def step(n, u):
                if has(n, BATCHES):
                    if not isinstance(n, int) or n >= 2:
                        waits_of_buffer(sp, stored, 0, n - 2, u)
                    sp.dma_start(rest[:, u], rows_of(g.skip2_rows, n)).then_inc(loaded[u], 16)
                k, v = n - 1, (u - 1) % 2
                if has(k, BATCHES):
                    evac.wait(sp, k * ROWS_B + (ROWS_B - 1))
                    sp.dma_start(rows_of(t["out"], k), rest[:, v]).then_inc(stored[v], 16)
            rolled(sp, BATCHES, 2, 1, step)
            for v in range(2):
                sp.wait_ge(stored[v], 16 * BATCHES // 2)

        @block.vector
        def _(dve):
            def step(n, u):
                if has(n, BATCHES):
                    D_["turned"].wait(dve, n - 2)
                    V.tensor_copy(sums[:, u], acc[:, ds(n * ROWS_B, ROWS_B), :]).then_inc(D_["acc_read"].sem, 1)
                    D_["acc_read"].wait(dve, n)
                    V.tensor_scalar(den[:, u].unsqueeze(2), sums[:, u, :, ACC_W - 1:ACC_W], DEN_EPS, None, ALU.add)\
                     .then_inc(D_["den"].sem, 1)
                    D_["den"].wait(dve, n)
                    V.reciprocal(den[:, u], den[:, u]).then_inc(D_["extra"].sem, 1)
                k, v = n - 1, (u - 1) % 2
                if has(k, BATCHES):
                    waits_of_buffer(dve, loaded, 0, k, v)
                    D_["extra"].wait(dve, k)
                    for j in range(ROWS_B):
                        D_["product"].wait(dve, k * ROWS_B + j)
                        V.scalar_tensor_tensor(out=rest[:, v, j], in0=ps_z[j % 4][:, 0:D],
                                               scalar=den[:, v, j:j + 1], in1=rest[:, v, j],
                                               op0=ALU.mult, op1=ALU.add).then_inc(evac.sem, 1)
            rolled(dve, BATCHES, 2, 1, step)

        @block.tensor
        def _(pe):
            pe.wait_ge(s_w, 48)

            def step(n, u):
                D_["acc_read"].wait(pe, n)
                D_["turned_sb"].wait(pe, n - 1)
                for j in range(ROWS_B):
                    T_.transpose(ps_h[:, j], sums[:, u, j, 0:D], ident[:])
                    i = T_.transpose(ps_t[0:TAIL, j], sums[:, u, j, D:ACC_W], ident[:])
                i.then_inc(D_["turned"].sem, 1)
                D_["turned_sb"].wait(pe, n)
                for j in range(ROWS_B):
                    evac.wait(pe, n * ROWS_B + (j - 3))
                    T_.matmul(ps_z[j % 4][:, 0:D], sT[:, j], wv[:], start=True, stop=False)
                    T_.matmul(ps_z[j % 4][:, 0:D], tT[:, j], wt[:], start=False, stop=True)\
                      .then_inc(D_["product"].sem, 1)
            rolled(pe, BATCHES, 2, 0, step)

        @block.scalar
        def _(act):
            def step(n, u):
                D_["turned"].wait(act, n)
                D_["product"].wait(act, n * ROWS_B - 1)
                S_.activation(sT[:], ps_h[:, 0:ROWS_B], ACT.Copy)
                S_.activation(tT[:], ps_t[0:TAIL, 0:ROWS_B], ACT.Copy).then_inc(D_["turned_sb"].sem, 1)
            rolled(act, BATCHES, 2, 0, step)


def host(inputs):
    import numpy as np
    a = {k: np.ascontiguousarray(v) for k, v in inputs.items()}
    x = np.zeros((NODES, D), a["x"].dtype)
    x[:N_NODES] = a["x"]
    src = np.zeros(EDGE_TILES * P, a["src"].dtype)
    src[:N_EDGES] = a["src"]
    dst = np.full(EDGE_TILES * P, PAD_DST, a["dst"].dtype)
    dst[:N_EDGES] = a["dst"]
    ea = np.zeros((EDGES, EDGE_DIM), a["edge_attr_16"].dtype)
    ea[:N_EDGES] = a["edge_attr_16"]
    a.update(x=x, src=src.reshape(EDGE_TILES, P), dst=dst.reshape(EDGE_TILES, P), edge_attr_16=ea)
    return a


def kernel(**inputs):
    import concourse.bacc as bacc
    from concourse.bass_utils import run_bass_kernel_spmd

    arrays = host(inputs)
    nc = bacc.Bacc("TRN2", target_bir_lowering=False, num_devices=1)
    t = {k: nc.dram_tensor("in_" + k, v.shape, mybir.dt.from_np(v.dtype), kind="ExternalInput").ap()
         for k, v in arrays.items()}
    t["out"] = nc.dram_tensor("out", [NODES, D], F32, kind="ExternalOutput").ap()
    build(nc, t)
    got = run_bass_kernel_spmd(nc, [{"in_" + k: v for k, v in arrays.items()}], core_ids=[0])
    return got.results[0]["out"][:N_NODES]
```
